# Optimizing a Trainium2 kernel written in Bass

```python
import numpy as np
import jax
import jax.numpy as jnp

def _softmax(x, axis=-1):
    return jax.nn.softmax(x, axis=axis)

def _gelu(x):
    return jax.nn.gelu(x, approximate=True)

def _silu(x):
    return jax.nn.silu(x)

def _sigmoid(x):
    return jax.nn.sigmoid(x)

def _layernorm(x, axis=-1, eps=1e-05):
    m = jnp.mean(x, axis=axis, keepdims=True)
    v = jnp.var(x, axis=axis, keepdims=True)
    return (x - m) / jnp.sqrt(v + eps)

def _scatter_add(tgt, idx, src, axis=0):
    return tgt.at[idx].add(src)

def _segment_sum(src, seg, n):
    return jax.ops.segment_sum(src, seg, n)
kernel_name = 'mk_adj_resnorm_d1_adj_r2_75c012'

def setup_inputs(seed: int=0):
    np.random.seed(seed)
    _w = jnp.asarray

    def _rec_inputs():
        import jax
        import jax.numpy as jnp
        _gk = jax.random.key(seed)
        x = 0.0002279 + 0.9999 * jax.random.normal(jax.random.fold_in(_gk, 1), (8192, 128), jnp.float32)
        _a = jax.random.bernoulli(jax.random.fold_in(_gk, 2), 0.000488281, (8192, 8192))
        adj = _a.astype(jnp.int32)
        return (x, adj)
    x, adj = _rec_inputs()

    def _L0_gnn_setup():
        import jax, jax.numpy as jnp
        import numpy as np
        N = 4096
        IN_F = 128
        OUT_F = 128
        ALPHA = 0.2
        NEG_FILL = -9000000000000000.0
        key = jax.random.key(seed)
        k_adj, k_h, k_w, k_a = jax.random.split(key, 4)
        adj = jax.random.randint(k_adj, (N, N), 0, 2, dtype=jnp.int32)
        h = jax.random.normal(k_h, (N, IN_F), dtype=jnp.float32)
        W = jax.random.normal(k_w, (IN_F, OUT_F), dtype=jnp.float32) * (2.0 / (IN_F + OUT_F)) ** 0.5
        a = jax.random.normal(k_a, (2 * OUT_F, 1), dtype=jnp.float32) * (2.0 / (2 * OUT_F + 1)) ** 0.5
        return {'adj': adj, 'h': h, 'W': W, 'a': a}
    _L0_gnn_all = _L0_gnn_setup()
    _L0_gnn_in = {k: v for k, v in _L0_gnn_all.items() if k in ('W', 'a')}
    del _L0_gnn_all
    return {'x': x, 'adj': adj, 'L0_gnn_W': _L0_gnn_in['W'], 'L0_gnn_a': _L0_gnn_in['a']}

def reference(x, adj, L0_gnn_W, L0_gnn_a):
    import jax
    import jax.numpy as jnp

    def _L0_gnn_ref(adj, h, W, a):
        import jax, jax.numpy as jnp
        import numpy as np
        N = 4096
        IN_F = 128
        OUT_F = 128
        ALPHA = 0.2
        NEG_FILL = -9000000000000000.0
        Wh = h @ W
        Wh1 = Wh @ a[:OUT_F, :]
        Wh2 = Wh @ a[OUT_F:, :]
        e = jax.nn.leaky_relu(Wh1 + Wh2.T, ALPHA)
        attention = jnp.where(adj > 0, e, jnp.float32(NEG_FILL))
        attention = jax.nn.softmax(attention, axis=1)
        h_prime = attention @ Wh
        return jax.nn.elu(h_prime)
    x = _layernorm(x + _L0_gnn_ref(adj, x, L0_gnn_W, L0_gnn_a), axis=-1)
    return x

_drawn_inputs = setup_inputs


def setup_inputs(seed=0):
    import zlib

    import numpy as np

    out = dict(_drawn_inputs(seed))
    spreads = {}
    factors = {}
    for name, (base, spread) in spreads.items():
        noise = np.random.default_rng([zlib.crc32(name.encode()), seed]).standard_normal(out[name].shape)
        drawn = base * np.exp(spread * noise) if base else spread * noise
        out[name] = jnp.asarray(drawn.astype(out[name].dtype))
    for name, factor in factors.items():
        out[name] = (out[name] * factor).astype(out[name].dtype)
    return out
```

```python
from contextlib import ExitStack

import concourse.bass as bass
from concourse import mybir

ALU = mybir.AluOpType
ACT = mybir.ActivationFunctionType
AX = mybir.AxisListType
F32 = mybir.dt.float32
BF16 = mybir.dt.bfloat16
I32 = mybir.dt.int32
RMAX = bass.bass_isa.ReduceOp.max

P = 128
ALPHA = 0.2
EPS = 1e-05


def gat_norm(nc, adj_t, x_t, x, w, w_t, a_t, out):
    N, F = x.shape
    JT = N // P
    IT = 4
    GW = IT * P
    G = N // GW
    CJ = adj_t.shape[2] // GW
    C = JT // CJ
    R = 4
    SW = C // R
    FV = F + 1
    BANK = 512
    HALF = 2

    with ExitStack() as ctx:
        def sb(name, shape, dt=F32):
            return ctx.enter_context(nc.sbuf_tensor(name, shape, dt))

        def sem(name):
            return ctx.enter_context(nc.semaphore(name))

        adj_ring = sb("adj_ring", [P, R, CJ, GW], I32)
        edge_ring = sb("edge_ring", [P, R, CJ, GW], BF16)
        wgt_ring = sb("wgt_ring", [P, R, CJ, GW])
        gamma = sb("gamma", [P, G, GW])
        vals = sb("vals", [P, JT, FV])
        beta = sb("beta", [P, JT])
        w_ext = sb("w_ext", [P, FV])
        w_tr = sb("w_tr", [P, F])
        a_sb = sb("a_sb", [P, 2])
        a_cols = sb("a_cols", [P, FV])
        wa1 = sb("wa1", [P, P])
        tmax_p = sb("tmax_p", [P, 1])
        tmax = sb("tmax", [P, 1])
        neg8 = sb("neg8", [P, 1])
        neg2 = sb("neg2", [P, 1])
        eps_sb = sb("eps_sb", [P, 1])
        xsum4 = sb("xsum4", [P, R])
        xsum = sb("xsum", [P, 1])
        xmean = sb("xmean", [P, P])
        wh_mean = sb("wh_mean", [P, 1, F])
        x_in = sb("x_in", [P, IT, F])
        lone = sb("lone", [P, IT, 1])
        den = sb("den", [P, IT, 1])
        rden = sb("rden", [P, IT, 1])
        agg = sb("agg", [P, IT, F])
        unif = sb("unif", [P, IT, F])
        neg = sb("neg", [P, IT, F])
        expd = sb("expd", [P, IT, F])
        res = sb("res", [P, IT, F])
        stats = sb("stats", [P, IT, 6])
        mdif = sb("mdif", [P, IT, 1])
        msum = sb("msum", [P, IT, 1])
        vsum = sb("vsum", [P, IT, 1])
        mean = sb("mean", [P, IT, 1])
        sdev = sb("sdev", [P, IT, 1])
        rstd = sb("rstd", [P, IT, 1])
        y_out = sb("y_out", [P, IT, F])
        psum = ctx.enter_context(nc.psum_tensor("psum", [P, 8, BANK], F32))

        xt_flat = wgt_ring[:, :, :, :].rearrange("p r q i -> p (r q i)")

        s_small = sem("s_small")
        s_xt = [sem(f"s_xt{r}") for r in range(R)]
        s_adj = [sem(f"s_adj{r}") for r in range(R)]
        s_eps = sem("s_eps")
        s_acols = sem("s_acols")
        s_wa = sem("s_wa")
        s_wasb = sem("s_wasb")
        s_wh = sem("s_wh")
        s_wh_dve = sem("s_wh_dve")
        s_wh_act = sem("s_wh_act")
        s_s = sem("s_s")
        s_sclip = sem("s_sclip")
        s_gamma = sem("s_gamma")
        s_tp = sem("s_tp")
        s_tmax = sem("s_tmax")
        s_neg = sem("s_neg")
        s_beta = sem("s_beta")
        s_vals = sem("s_vals")
        s_xs = sem("s_xs")
        s_xsum = sem("s_xsum")
        s_mean = sem("s_mean")
        s_meansb = sem("s_meansb")
        s_edge = sem("s_edge")
        s_wgt = sem("s_wgt")
        s_used = sem("s_used")
        s_bank = sem("s_bank")
        s_epi = sem("s_epi")
        s_neg_h = sem("s_neg_h")
        s_exp = sem("s_exp")
        s_var = sem("s_var")
        s_sd = sem("s_sd")
        s_rstd = sem("s_rstd")
        s_xin = sem("s_xin")
        s_xused = sem("s_xused")
        s_y = sem("s_y")
        s_out = sem("s_out")
        s_yfree = sem("s_yfree")

        x_rows = x.rearrange("(g t p) f -> g p t f", t=IT, p=P)
        out_rows = out.rearrange("(g t p) f -> g p t f", t=IT, p=P)

        block = ctx.enter_context(nc.Block())

        @block.sync
        def _(sp):
            sp.dma_start(w_ext[:, 0:F], w).then_inc(s_small, 16)
            sp.dma_start(w_tr[:, :], w_t).then_inc(s_small, 16)
            sp.dma_start(a_sb[:, :], a_t).then_inc(s_small, 16)
            for r in range(R):
                sp.dma_start(xt_flat[:, r * CJ * GW:(r + 1) * CJ * GW],
                             x_t[:, r * CJ * GW:(r + 1) * CJ * GW]).then_inc(s_xt[r], 16)
            for r in range(R):
                sp.dma_start(adj_ring[:, r].rearrange("p q i -> p (q i)"), adj_t[r]).then_inc(s_adj[r], 16)
            with sp.Fori(1, G * SW) as k:
                for r in range(R):
                    sp.wait_ge(s_edge, k * R + (r + 1 - R))
                    sp.dma_start(adj_ring[:, r].rearrange("p q i -> p (q i)"),
                                 adj_t[bass.ds(k * R + r, 1)].rearrange("o p n -> (o p) n")).then_inc(s_adj[r], 16)

        @block.gpsimd
        def _(pool):
            pool.sem_inc(s_yfree, 1)
            pool.wait_ge(s_tp, 1)
            nc.gpsimd.partition_all_reduce(tmax[:, :], tmax_p[:, :], P, RMAX).then_inc(s_tmax, 1)
            pool.dma_start(x_in[:, :, :], x_rows[0]).then_inc(s_xin, 16)
            with pool.Fori(0, G - 1) as g:
                pool.wait_ge(s_xused, g + 1)
                pool.dma_start(x_in[:, :, :], x_rows[bass.ds(g + 1, 1)].rearrange("o p t f -> (o p) t f")
                               ).then_inc(s_xin, 16)
                pool.wait_ge(s_y, g + 1)
                pool.dma_start(out_rows[bass.ds(g, 1)].rearrange("o p t f -> (o p) t f"), y_out[:, :, :]
                               ).then_inc(s_out, 16)
                pool.wait_ge(s_out, g * 16 + 16)
                pool.sem_inc(s_yfree, 1)
            pool.wait_ge(s_y, G)
            pool.dma_start(out_rows[G - 1], y_out[:, :, :]).then_inc(s_out, 16)
            pool.wait_ge(s_out, 16 * G)

        @block.scalar
        def _(act):
            for r in range(R):
                act.wait_ge(s_xt[r], 16)
                nc.scalar.activation(edge_ring[:, r].rearrange("p q i -> p (q i)"),
                                     xt_flat[:, r * CJ * GW:(r + 1) * CJ * GW], ACT.Copy,
                                     accum_out=xsum4[:, r:r + 1]).then_inc(s_xs, 1)
                for b in range(4 * r + 1, 4 * r + 4, 2):
                    act.wait_ge(s_wh, b + 1)
                    nc.scalar.copy(vals[:, 4 * b:4 * b + 4, :].rearrange("p (k h) f -> p k (h f)", h=HALF),
                                   psum[:, 2:4, 0:HALF * FV]).then_inc(s_wh_act, 1)
            act.wait_ge(s_neg, 2)
            nc.scalar.activation(beta[:, :], vals[:, :, F], ACT.Exp, bias=neg8[:, :],
                                 scale=1 - ALPHA).then_inc(s_beta, 1)
            act.wait_ge(s_beta, 1)
            nc.scalar.activation(vals[:, :, F], vals[:, :, F], ACT.Exp, bias=neg2[:, :],
                                 scale=ALPHA).then_inc(s_beta, 1)
            for g in range(G):
                act.wait_ge(s_sclip, g + 1)
                nc.scalar.activation(gamma[:, g, :], gamma[:, g, :], ACT.Exp,
                                     scale=-(1 - ALPHA)).then_inc(s_gamma, 1)

            def edges(k):
                for r in range(R):
                    act.wait_ge(s_adj[r], k * 16 + 16)
                    if not (isinstance(k, int) and k == 0):
                        act.wait_ge(s_wgt, k * R + (r + 1 - R))
                    nc.scalar.activation(edge_ring[:, r].rearrange("p q i -> p (q i)"),
                                         adj_ring[:, r].rearrange("p q i -> p (q i)"), ACT.Relu).then_inc(s_edge, 1)

            def epilogue(g):
                act.wait_ge(s_neg_h, g + 1)
                nc.scalar.activation(expd[:, :, :], neg[:, :, :], ACT.Exp).then_inc(s_exp, 1)
                act.wait_ge(s_var, g + 1)
                nc.scalar.activation(sdev[:, :, :], vsum[:, :, :], ACT.Sqrt, bias=eps_sb[:, :], scale=1.0 / F).then_inc(s_sd, 1)

            edges(0)
            with act.Fori(1, SW) as k:
                edges(k)
            with act.Fori(0, G - 1) as g:
                edges((g + 1) * SW)
                epilogue(g)
                with act.Fori(1, SW) as k:
                    edges((g + 1) * SW + k)
            epilogue(G - 1)

        @block.vector
        def _(dve):
            nc.vector.memset(eps_sb[:, :], EPS).then_inc(s_eps, 1)
            dve.wait_ge(s_small, 48)
            nc.vector.tensor_copy(a_cols[:, 0:P], a_sb[:, 0:1].to_broadcast([P, P])).then_inc(s_acols, 1)
            nc.vector.tensor_copy(a_cols[:, P:FV], a_sb[:, 1:2]).then_inc(s_acols, 1)
            dve.wait_ge(s_wa, 1)
            nc.vector.tensor_copy(wa1[:, :], psum[:, 4, 0:P]).then_inc(s_wasb, 1)
            nc.vector.tensor_copy(w_ext[:, F:FV], psum[:, 4, P:FV]).then_inc(s_wasb, 1)
            for b in range(0, JT // 4, 2):
                dve.wait_ge(s_wh, b + 1)
                nc.vector.tensor_copy(vals[:, 4 * b:4 * b + 4, :].rearrange("p (k h) f -> p k (h f)", h=HALF),
                                      psum[:, 0:2, 0:HALF * FV]).then_inc(s_wh_dve, 1)
            dve.wait_ge(s_wh_dve, JT // 8)
            dve.wait_ge(s_wh_act, JT // 8)
            nc.vector.tensor_reduce(tmax_p[:, :], vals[:, :, F], AX.X, ALU.max).then_inc(s_tp, 1)
            dve.wait_ge(s_xs, R)
            nc.vector.tensor_reduce(xsum[:, :], xsum4[:, :], AX.X, ALU.add).then_inc(s_xsum, 1)
            dve.wait_ge(s_xsum, 1)
            nc.vector.tensor_scalar(xmean[:, :], xsum[:, 0:1].to_broadcast([P, P]), 1.0 / N, None,
                                    ALU.mult).then_inc(s_xsum, 1)
            dve.wait_ge(s_tmax, 1)
            nc.vector.tensor_scalar(neg8[:, :], tmax[:, :], -(1 - ALPHA), None, ALU.mult).then_inc(s_neg, 1)
            nc.vector.tensor_scalar(neg2[:, :], tmax[:, :], -ALPHA, None, ALU.mult).then_inc(s_neg, 1)
            for g in range(G):
                dve.wait_ge(s_s, g + 1)
                nc.vector.tensor_scalar(gamma[:, g, :], psum[:, 4 + g % 4, :], tmax[:, 0:1], 0.0,
                                        ALU.add, ALU.max).then_inc(s_sclip, 1)
            dve.wait_ge(s_beta, 2)
            nc.vector.tensor_tensor(vals[:, :, 0:F], vals[:, :, 0:F],
                                    vals[:, :, F:FV].to_broadcast([P, JT, F]), ALU.mult).then_inc(s_vals, 1)
            dve.wait_ge(s_mean, 1)
            nc.vector.tensor_copy(wh_mean[:, 0, :], psum[:, 0, 0:F]).then_inc(s_bank, 2)
            dve.wait_ge(s_gamma, G)

            def weights(g, sweep):
                for r in range(R):
                    c = g * C + sweep * R + r
                    dve.wait_ge(s_edge, c + 1)
                    dve.wait_ge(s_used, c + 1)
                    for q in range(CJ):
                        jt = sweep * R * CJ + r * CJ + q
                        gam = gamma[:, g, :] if isinstance(g, int) else \
                            gamma[:, bass.ds(g, 1), :].rearrange("p o i -> p (o i)")
                        bet = beta[:, jt:jt + 1] if isinstance(jt, int) else beta[:, bass.ds(jt, 1)]
                        op = nc.vector.scalar_tensor_tensor(
                            out=wgt_ring[:, r, q, :], in0=gam, scalar=bet, in1=edge_ring[:, r, q, :],
                            op0=ALU.max, op1=ALU.min)
                    op.then_inc(s_wgt, 1)

            STEPS = 13

            def epilogue(g, par):
                b0 = 4 * par
                num = psum[:, b0:b0 + IT, 0:F]
                dps = psum[:, b0:b0 + IT, F:FV]
                e0 = g * STEPS
                dve.wait_ge(s_used, (g + 1) * C + R)
                nc.vector.tensor_scalar(lone[:, :, :], dps, 0.0, None, ALU.is_equal).then_inc(s_epi, 1)
                dve.wait_ge(s_epi, e0 + 1)
                nc.vector.tensor_tensor(den[:, :, :], dps, lone[:, :, :], ALU.add).then_inc(s_epi, 1)
                dve.wait_ge(s_epi, e0 + 2)
                nc.vector.reciprocal(rden[:, :, :], den[:, :, :]).then_inc(s_epi, 1)
                dve.wait_ge(s_epi, e0 + 3)
                nc.vector.tensor_tensor(agg[:, :, :], num, rden[:, :, :].to_broadcast([P, IT, F]),
                                        ALU.mult).then_inc(s_bank, 1)
                nc.vector.tensor_tensor(unif[:, :, :], wh_mean[:, :, :].to_broadcast([P, IT, F]),
                                        lone[:, :, :].to_broadcast([P, IT, F]), ALU.mult).then_inc(s_epi, 1)
                dve.wait_ge(s_epi, e0 + 4)
                dve.wait_ge(s_bank, g + 3)
                nc.vector.tensor_tensor(agg[:, :, :], agg[:, :, :], unif[:, :, :], ALU.add).then_inc(s_epi, 1)
                dve.wait_ge(s_epi, e0 + 5)
                nc.vector.tensor_scalar(neg[:, :, :], agg[:, :, :], 0.0, None, ALU.min).then_inc(s_neg_h, 1)
                dve.wait_ge(s_xin, g * 16 + 16)
                nc.vector.tensor_scalar(agg[:, :, :], agg[:, :, :], 0.0, -1.0, ALU.max, ALU.add).then_inc(s_epi, 1)
                dve.wait_ge(s_epi, e0 + 6)
                nc.vector.tensor_tensor(agg[:, :, :], agg[:, :, :], x_in[:, :, :], ALU.add).then_inc(s_xused, 1)
                dve.wait_ge(s_xused, g + 1)
                dve.wait_ge(s_exp, g + 1)
                nc.vector.tensor_tensor(res[:, :, :], agg[:, :, :], expd[:, :, :], ALU.add).then_inc(s_epi, 1)
                dve.wait_ge(s_epi, e0 + 7)
                for t in range(IT):
                    op = nc.vector.bn_stats(stats[:, t, :], res[:, t, :])
                op.then_inc(s_epi, 1)
                dve.wait_ge(s_epi, e0 + 8)
                nc.vector.tensor_tensor(mdif[:, :, :], stats[:, :, 1:2], stats[:, :, 4:5], ALU.subtract).then_inc(s_epi, 1)
                nc.vector.tensor_tensor(msum[:, :, :], stats[:, :, 1:2], stats[:, :, 4:5], ALU.add).then_inc(s_epi, 1)
                nc.vector.tensor_tensor(vsum[:, :, :], stats[:, :, 2:3], stats[:, :, 5:6], ALU.add).then_inc(s_epi, 1)
                dve.wait_ge(s_epi, e0 + 11)
                nc.vector.scalar_tensor_tensor(out=mdif[:, :, :], in0=mdif[:, :, :], scalar=F / 4, in1=mdif[:, :, :],
                                               op0=ALU.mult, op1=ALU.mult).then_inc(s_epi, 1)
                nc.vector.tensor_scalar(mean[:, :, :], msum[:, :, :], 0.5, None, ALU.mult).then_inc(s_epi, 1)
                dve.wait_ge(s_epi, e0 + 13)
                nc.vector.tensor_tensor(vsum[:, :, :], vsum[:, :, :], mdif[:, :, :], ALU.add).then_inc(s_var, 1)
                dve.wait_ge(s_sd, g + 1)
                nc.vector.reciprocal(rstd[:, :, :], sdev[:, :, :]).then_inc(s_rstd, 1)
                dve.wait_ge(s_rstd, g + 1)
                dve.wait_ge(s_yfree, g + 1)
                for t in range(IT):
                    op = nc.vector.tensor_scalar(y_out[:, t, :], res[:, t, :], mean[:, t, 0:1], rstd[:, t, 0:1],
                                                 ALU.subtract, ALU.mult)
                op.then_inc(s_y, 1)

            weights(0, 0)
            with dve.Fori(1, SW) as k:
                weights(0, k)
            with dve.Fori(0, G // 2 - 1) as m:
                for par in range(2):
                    weights(m * 2 + (par + 1), 0)
                    epilogue(m * 2 + par, par)
                    with dve.Fori(1, SW) as k:
                        weights(m * 2 + (par + 1), k)
            weights(G - 1, 0)
            epilogue(G - 2, 0)
            with dve.Fori(1, SW) as k:
                weights(G - 1, k)
            epilogue(G - 1, 1)

        @block.tensor
        def _(pe):
            pe.wait_ge(s_small, 48)
            pe.wait_ge(s_acols, 2)
            nc.tensor.matmul(psum[:, 4, 0:FV], w_tr[:, :], a_cols[:, :], start=True, stop=True).then_inc(s_wa, 1)
            pe.wait_ge(s_wasb, 2)
            for b in range(JT // 4):
                if b % 4 == 0:
                    pe.wait_ge(s_xt[b // 4], 16)
                if b >= 2:
                    pe.wait_ge([s_wh_dve, s_wh_act][b % 2], b // 2)
                for q in range(4):
                    jt = 4 * b + q
                    bank = 2 * (b % 2) + q // HALF
                    op = nc.tensor.matmul(psum[:, bank, (q % HALF) * FV:(q % HALF + 1) * FV],
                                          xt_flat[:, jt * P:(jt + 1) * P], w_ext[:, :], start=True, stop=True)
                op.then_inc(s_wh, 1)
            for g in range(G):
                if g >= 4:
                    pe.wait_ge(s_sclip, g - 3)
                op = nc.tensor.matmul(psum[:, 4 + g % 4, :], wa1[:, :], xt_flat[:, g * GW:(g + 1) * GW],
                                      start=True, stop=True)
                op.then_inc(s_s, 1)
            pe.wait_ge(s_xsum, 2)
            pe.wait_ge(s_wh_dve, JT // 8)
            nc.tensor.matmul(psum[:, 0, 0:F], xmean[:, :], w_ext[:, 0:F], start=True, stop=True).then_inc(s_mean, 1)
            pe.wait_ge(s_vals, 1)
            pe.sem_inc(s_used, R)

            def products(g, par, sweep):
                for r in range(R):
                    pe.wait_ge(s_wgt, g * C + sweep * R + (r + 1))
                    for q in range(CJ):
                        jt = sweep * (R * CJ) + (r * CJ + q)
                        first = isinstance(jt, int) and jt == 0
                        last = isinstance(jt, int) and jt == JT - 1
                        v = vals[:, jt, :] if isinstance(jt, int) else \
                            vals[:, bass.ds(jt, 1), :].rearrange("p o f -> p (o f)")
                        for t in range(IT):
                            op = nc.tensor.matmul(psum[:, 4 * par + t, 0:FV], wgt_ring[:, r, q, t * P:(t + 1) * P], v,
                                                  start=first, stop=last)
                    op.then_inc(s_used, 1)

            with pe.Fori(0, G // 2) as m:
                for par in range(2):
                    pe.wait_ge(s_bank, m * 2 + (par + 1))
                    products(m * 2 + par, par, 0)
                    with pe.Fori(1, SW - 1) as k:
                        products(m * 2 + par, par, k)
                    products(m * 2 + par, par, SW - 1)


def kernel(x, adj, L0_gnn_W, L0_gnn_a):
    import numpy as np
    import concourse.bacc as bacc
    from concourse.bass_utils import run_bass_kernel_spmd

    x = np.ascontiguousarray(x)
    adj = np.asarray(adj)
    w = np.ascontiguousarray(L0_gnn_W)
    n = x.shape[0]
    rows, tiles = 512, 4
    adj_t = adj.reshape(n // rows, rows, n // (tiles * 128), tiles, 128).transpose(0, 2, 4, 3, 1)
    arrays = {
        "adj_t": np.ascontiguousarray(adj_t).reshape(-1, 128, tiles * rows),
        "x_t": np.ascontiguousarray(x.T),
        "x": x,
        "w": w,
        "w_t": np.ascontiguousarray(w.T),
        "a_t": np.ascontiguousarray(np.asarray(L0_gnn_a).reshape(2, -1).T),
    }
    nc = bacc.Bacc("TRN2", target_bir_lowering=False, num_devices=1)
    args = [nc.dram_tensor(k, v.shape, mybir.dt.from_np(v.dtype), kind="ExternalInput").ap()
            for k, v in arrays.items()]
    out = nc.dram_tensor("out", x.shape, F32, kind="ExternalOutput").ap()
    gat_norm(nc, *args, out)
    r = run_bass_kernel_spmd(nc, [arrays], core_ids=[0])
    return r.results[0]["out"]
```

```python
from contextlib import ExitStack

import concourse.bass as bass
from concourse import mybir

ALU = mybir.AluOpType
ACT = mybir.ActivationFunctionType
AX = mybir.AxisListType
F32 = mybir.dt.float32
BF16 = mybir.dt.bfloat16
I32 = mybir.dt.int32
RMAX = bass.bass_isa.ReduceOp.max

P = 128
ALPHA = 0.2
EPS = 1e-05


def gat_norm(nc, adj_t, x_t, x, w, w_t, a_t, out):
    N, F = x.shape
    JT = N // P
    IT = 4
    GW = IT * P
    G = N // GW
    CJ = adj_t.shape[2] // GW
    C = JT // CJ
    R = 4
    SW = C // R
    FV = F + 1
    FX = F + 2
    XD = 8
    XA = 2
    FOLDS = [512, 256, 128]
    WH_BANKS = [0, 2, 5]
    BANK = 512
    HALF = 2

    with ExitStack() as ctx:
        def sb(name, shape, dt=F32):
            return ctx.enter_context(nc.sbuf_tensor(name, shape, dt))

        def sem(name):
            return ctx.enter_context(nc.semaphore(name))

        adj_ring = sb("adj_ring", [P, R, CJ, GW], I32)
        edge_ring = sb("edge_ring", [P, R, CJ, GW], BF16)
        wgt_ring = sb("wgt_ring", [P, R, CJ, GW])
        gamma = sb("gamma", [P, 2, GW])
        gamma_rows = sb("gamma_rows", [JT, P])
        vals = sb("vals", [P, JT, FX])
        beta = sb("beta", [P, JT])
        clip = sb("clip", [P, JT])
        w_ext = sb("w_ext", [P, FX])
        w_tr = sb("w_tr", [P, F])
        a_sb = sb("a_sb", [P, 2])
        wa1 = sb("wa1", [P, P])
        ident = sb("ident", [P, P])
        ones = sb("ones", [1, P])
        tmax_p = sb("tmax_p", [P, 1])
        tmax_1 = sb("tmax_1", [1, 1])
        tmax = sb("tmax", [P, 3])
        eps_sb = sb("eps_sb", [P, 1])
        xfold = sb("xfold", [P, XA + N // XD])
        xsum = sb("xsum", [P, 1])
        xmean = sb("xmean", [P, P])
        wh_mean = sb("wh_mean", [P, 1, F])
        x_in = sb("x_in", [P, IT, F])
        lone = sb("lone", [P, IT, 1])
        den = sb("den", [P, IT, 1])
        rden = sb("rden", [P, IT, 1])
        agg = sb("agg", [P, IT, F])
        unif = sb("unif", [P, IT, F])
        neg = sb("neg", [P, IT, F])
        expd = sb("expd", [P, IT, F])
        res = sb("res", [P, IT, F])
        stats = sb("stats", [P, IT, 6])
        mdif = sb("mdif", [P, IT, 1])
        msum = sb("msum", [P, IT, 1])
        vsum = sb("vsum", [P, IT, 1])
        mean = sb("mean", [P, IT, 1])
        sdev = sb("sdev", [P, IT, 1])
        rstd = sb("rstd", [P, IT, 1])
        y_out = sb("y_out", [P, IT, F])
        psum = ctx.enter_context(nc.psum_tensor("psum", [P, 8, BANK], F32))
        gamma_dram = nc.dram_tensor("gamma_dram", [JT, P], F32, kind="Internal").ap()
        gamma_groups = gamma_dram.rearrange("(g t) p -> g (t p)", t=IT)

        xt_flat = wgt_ring[:, :, :, :].rearrange("p r q i -> p (r q i)")
        XC = N // XD
        SLOT = CJ * GW

        s_small = sem("s_small")
        s_xt = [sem(f"s_xt{r}") for r in range(XD)]
        s_adj = [sem(f"s_adj{r}") for r in range(R)]
        s_const = sem("s_const")
        s_id0 = sem("s_id0")
        s_ident = sem("s_ident")
        s_wa = sem("s_wa")
        s_wasb = sem("s_wasb")
        s_wh = sem("s_wh")
        s_wh_dve = sem("s_wh_dve")
        s_wh_act = sem("s_wh_act")
        s_s0 = sem("s_s0")
        s_clip = sem("s_clip")
        s_clip_t = sem("s_clip_t")
        s_gamma0 = sem("s_gamma0")
        s_gamma_row = sem("s_gamma_row")
        s_gamma_st = sem("s_gamma_st")
        s_gamma = sem("s_gamma")
        s_tp = sem("s_tp")
        s_tpt = sem("s_tpt")
        s_t1 = sem("s_t1")
        s_tb = sem("s_tb")
        s_tmax = sem("s_tmax")
        s_beta = sem("s_beta")
        s_vals = sem("s_vals")
        s_xs = sem("s_xs")
        s_xs_act = sem("s_xs_act")
        s_xsum = sem("s_xsum")
        s_mean = sem("s_mean")
        s_edge = sem("s_edge")
        s_wgt = sem("s_wgt")
        s_used = sem("s_used")
        s_bank = [sem(f"s_bank{p}") for p in range(2)]
        s_epi = sem("s_epi")
        s_neg_h = sem("s_neg_h")
        s_exp = sem("s_exp")
        s_var = sem("s_var")
        s_sd = sem("s_sd")
        s_rstd = sem("s_rstd")
        s_xin = sem("s_xin")
        s_xused = sem("s_xused")
        s_y = sem("s_y")
        s_out = sem("s_out")
        s_last = [sem(f"s_last{k}") for k in range(2)]
        s_half = sem("s_half")
        s_yfree = sem("s_yfree")

        x_rows = x.rearrange("(g t p) f -> g p t f", t=IT, p=P)
        out_rows = out.rearrange("(g t p) f -> g p t f", t=IT, p=P)

        def wh_banks(b):
            first = WH_BANKS[b % len(WH_BANKS)]
            return psum[:, first:first + 2, 0:HALF * FX]

        block = ctx.enter_context(nc.Block())

        @block.sync
        def _(sp):
            sp.dma_start(w_tr[:, :], w_t).then_inc(s_small, 16)
            sp.dma_start(a_sb[:, :], a_t).then_inc(s_small, 16)
            sp.dma_start(w_ext[:, 0:F], w).then_inc(s_small, 16)
            for r in range(XD):
                sp.dma_start(xt_flat[:, r * XC:(r + 1) * XC], x_t[:, r * XC:(r + 1) * XC]).then_inc(s_xt[r], 16)
            for r in range(R):
                sp.dma_start(adj_ring[:, r].rearrange("p q i -> p (q i)"), adj_t[r]).then_inc(s_adj[r], 16)
            with sp.Fori(1, G * SW) as k:
                for r in range(R):
                    sp.wait_ge(s_edge, k * R + (r + 1 - R))
                    sp.dma_start(adj_ring[:, r].rearrange("p q i -> p (q i)"),
                                 adj_t[bass.ds(k * R + r, 1)].rearrange("o p n -> (o p) n")).then_inc(s_adj[r], 16)

        @block.gpsimd
        def _(pool):
            nc.gpsimd.memset(ident[:, :], 0.0).then_inc(s_id0, 1)
            pool.wait_ge(s_id0, 1)
            nc.gpsimd.affine_select(out=ident[:, :], in_=ident[:, :], compare_op=ALU.not_equal, fill=1.0, base=0,
                                    pattern=[[-1, P]], channel_multiplier=1).then_inc(s_ident, 1)
            pool.sem_inc(s_yfree, 1)
            fold = xfold[:, XA:XA + XC]
            pool.wait_ge(s_xt[XA], 16)
            pool.wait_ge(s_xt[XA + 1], 16)
            nc.gpsimd.tensor_tensor(fold, xt_flat[:, XA * XC:(XA + 1) * XC], xt_flat[:, (XA + 1) * XC:(XA + 2) * XC],
                                    ALU.add).then_inc(s_xs, 1)
            for k in range(XA + 2, XD):
                pool.wait_ge(s_xt[k], 16)
                pool.wait_ge(s_xs, k - XA - 1)
                nc.gpsimd.tensor_tensor(fold, fold, xt_flat[:, k * XC:(k + 1) * XC], ALU.add).then_inc(s_xs, 1)
            for k, half in enumerate(FOLDS):
                pool.wait_ge(s_xs, XD - XA - 1 + k)
                nc.gpsimd.tensor_tensor(fold[:, 0:half], fold[:, 0:half], fold[:, half:2 * half],
                                        ALU.add).then_inc(s_xs, 1)
            pool.dma_start(x_in[:, :, :], x_rows[0]).then_inc(s_xin, 16)
            pool.wait_ge(s_gamma_row, 1)
            pool.dma_start(gamma_dram, gamma_rows[:, :]).then_inc(s_gamma_st, 16)
            pool.wait_ge(s_gamma_st, 16)
            pool.dma_start(gamma[:, 1, :], gamma_groups[1].partition_broadcast(P)).then_inc(s_gamma, 16)

            def load_x(g):
                pool.wait_ge(s_xused, g)
                rows = x_rows[g] if isinstance(g, int) else x_rows[bass.ds(g, 1)].rearrange("o p t f -> (o p) t f")
                pool.dma_start(x_in[:, :, :], rows).then_inc(s_xin, 16)

            def stored(g):
                pool.wait_ge(s_out, g * 16 + 16)
                pool.sem_inc(s_yfree, 1)

            with pool.Fori(0, G // 2 - 1) as m:
                for par in range(2):
                    load_x(m * 2 + (par + 1))
                    pool.dma_start(gamma[:, par, :], gamma_groups[bass.ds(m * 2 + (par + 2), 1)].rearrange(
                        "o n -> (o n)").partition_broadcast(P)).then_inc(s_gamma, 16)
                    stored(m * 2 + par)
            load_x(G - 1)
            stored(G - 2)

        @block.scalar
        def _(act):
            def edges(c, r, first=False):
                act.wait_ge(s_adj[r], c * 16 + 16)
                if not first:
                    act.wait_ge(s_wgt, c * R + (r + 1 - R))
                nc.scalar.activation(edge_ring[:, r].rearrange("p q i -> p (q i)"),
                                     adj_ring[:, r].rearrange("p q i -> p (q i)"), ACT.Relu).then_inc(s_edge, 1)

            for b in range(1, JT // 4, 2):
                act.wait_ge(s_wh, b + 1)
                nc.scalar.copy(vals[:, 4 * b:4 * b + 4, :].rearrange("p (k h) f -> p k (h f)", h=HALF),
                               wh_banks(b)).then_inc(s_wh_act, 1)
                if b // 2 < XA:
                    act.wait_ge(s_xt[b // 2], 16)
                    nc.scalar.activation(edge_ring[:, R - 1 - b // 2].rearrange("p q i -> p (q i)")[:, 0:XC],
                                         xt_flat[:, b // 2 * XC:(b // 2 + 1) * XC], ACT.Copy,
                                         accum_out=xfold[:, b // 2:b // 2 + 1]).then_inc(s_xs_act, 1)
            edges(0, 0, True)
            act.wait_ge(s_tmax, 3)
            nc.scalar.activation(beta[:, :], vals[:, :, F], ACT.Exp, bias=tmax[:, 1:2],
                                 scale=1 - ALPHA).then_inc(s_beta, 1)
            act.wait_ge(s_beta, 1)
            nc.scalar.activation(vals[:, :, F], vals[:, :, F], ACT.Exp, bias=tmax[:, 2:3],
                                 scale=ALPHA).then_inc(s_beta, 1)
            act.wait_ge(s_clip, 1)
            nc.scalar.activation(gamma[:, 0, :], gamma[:, 0, :], ACT.Exp, scale=-(1 - ALPHA)).then_inc(s_gamma0, 1)
            act.wait_ge(s_clip_t, 1)
            nc.scalar.activation(gamma_rows[:, :], psum[0:JT, 6, 0:P], ACT.Exp,
                                 scale=-(1 - ALPHA)).then_inc(s_gamma_row, 1)
            act.wait_ge(s_xs_act, XA)
            for r in range(1, R):
                edges(0, r, True)
            with act.Fori(1, SW) as k:
                for r in range(R):
                    edges(k, r)

            def exp_h(n, ts=slice(0, IT)):
                act.wait_ge(s_neg_h, n + 1)
                nc.scalar.activation(expd[:, ts, :], neg[:, ts, :], ACT.Exp).then_inc(s_exp, 1)

            def sqrt_var(n, ts=slice(0, IT)):
                act.wait_ge(s_var, n + 1)
                nc.scalar.activation(sdev[:, ts, :], vsum[:, ts, :], ACT.Sqrt, bias=eps_sb[:, :],
                                     scale=1.0 / F).then_inc(s_sd, 1)

            with act.Fori(0, G - 1) as g:
                for sweep in range(SW):
                    for r in range(R):
                        edges((g + 1) * SW + sweep, r)
                    if sweep == 0:
                        exp_h(g)
                    if sweep == 1:
                        sqrt_var(g)
                act.wait_ge(s_y, g + 1)
                act.dma_start(out_rows[bass.ds(g, 1)].rearrange("o p t f -> (o p) t f"), y_out[:, :, :]
                              ).then_inc(s_out, 16)
            halves = [slice(0, IT // 2), slice(IT // 2, IT)]
            for k, ts in enumerate(halves):
                exp_h(G - 1 + k, ts)
            for k, ts in enumerate(halves):
                sqrt_var(G - 1 + k, ts)
            for k, ts in enumerate(halves):
                act.wait_ge(s_y, G + k)
                act.dma_start(out_rows[G - 1][:, ts, :], y_out[:, ts, :]).then_inc(s_last[k], 16)
            act.wait_ge(s_out, 16 * (G - 1))
            act.wait_ge(s_last[0], 16)
            act.wait_ge(s_last[1], 16)

        @block.vector
        def _(dve):
            nc.vector.memset(eps_sb[:, :], EPS).then_inc(s_const, 1)
            nc.vector.memset(ones[:, :], 1.0).then_inc(s_const, 1)
            dve.wait_ge(s_wa, 1)
            nc.vector.tensor_copy(w_ext[:, F:F + 1], psum[:, 4, 1:2]).then_inc(s_wasb, 1)
            nc.vector.tensor_copy(w_ext[:, F + 1:FX], psum[:, 4, 0:1]).then_inc(s_wasb, 1)
            nc.vector.tensor_copy(wa1[:, :], psum[:, 4, 0:1].to_broadcast([P, P])).then_inc(s_wasb, 1)
            for b in range(0, JT // 4, 2):
                dve.wait_ge(s_wh, b + 1)
                nc.vector.tensor_copy(vals[:, 4 * b:4 * b + 4, :].rearrange("p (k h) f -> p k (h f)", h=HALF),
                                      wh_banks(b)).then_inc(s_wh_dve, 1)
            dve.wait_ge(s_wh_dve, JT // 8)
            dve.wait_ge(s_wh_act, JT // 8)
            nc.vector.tensor_reduce(tmax_p[:, :], vals[:, :, F], AX.X, ALU.max).then_inc(s_tp, 1)
            dve.wait_ge(s_tpt, 1)
            nc.vector.tensor_reduce(tmax_1[:, :], psum[0:1, 6, 0:P], AX.X, ALU.max).then_inc(s_t1, 1)
            dve.wait_ge(s_tb, 1)
            nc.vector.tensor_scalar(tmax[:, 1:2], psum[:, 4, 0:1], -(1 - ALPHA), None, ALU.mult).then_inc(s_tmax, 1)
            nc.vector.tensor_scalar(tmax[:, 2:3], psum[:, 4, 0:1], -ALPHA, None, ALU.mult).then_inc(s_tmax, 1)
            nc.vector.tensor_copy(tmax[:, 0:1], psum[:, 4, 0:1]).then_inc(s_tmax, 1)
            dve.wait_ge(s_tmax, 3)
            dve.wait_ge(s_s0, 1)
            nc.vector.tensor_scalar(gamma[:, 0, :], psum[:, 7, :], tmax[:, 0:1], 0.0,
                                    ALU.add, ALU.max).then_inc(s_clip, 1)
            nc.vector.tensor_scalar(clip[:, :], vals[:, :, F + 1], tmax[:, 0:1], 0.0,
                                    ALU.add, ALU.max).then_inc(s_clip, 1)
            dve.wait_ge(s_xs_act, XA)
            dve.wait_ge(s_xs, XD - XA - 1 + len(FOLDS))
            nc.vector.tensor_reduce(xsum[:, :], xfold[:, 0:XA + FOLDS[-1]], AX.X, ALU.add).then_inc(s_xsum, 1)
            dve.wait_ge(s_xsum, 1)
            nc.vector.tensor_scalar(xmean[:, :], xsum[:, 0:1].to_broadcast([P, P]), 1.0 / N, None,
                                    ALU.mult).then_inc(s_xsum, 1)
            dve.wait_ge(s_beta, 2)

            def weights(g, par, sweep):
                for r in range(R):
                    c = g * C + sweep * R + r
                    if isinstance(g, int) and g == 0:
                        jts = slice((sweep * R + r) * CJ, (sweep * R + r + 1) * CJ)
                        nc.vector.tensor_tensor(vals[:, jts, 0:F], vals[:, jts, 0:F],
                                                vals[:, jts, F:F + 1].to_broadcast([P, CJ, F]),
                                                ALU.mult).then_inc(s_vals, 1)
                        dve.wait_ge(s_gamma0, 1)
                    dve.wait_ge(s_edge, c + 1)
                    dve.wait_ge(s_used, c + 1)
                    for q in range(CJ):
                        jt = (sweep * R + r) * CJ + q
                        op = nc.vector.scalar_tensor_tensor(
                            out=wgt_ring[:, r, q, :], in0=gamma[:, par, :], scalar=beta[:, jt:jt + 1], in1=edge_ring[:, r, q, :],
                            op0=ALU.max, op1=ALU.min)
                    op.then_inc(s_wgt, 1)

            HEAD_STEPS, BODY_STEPS = 6, 7
            STEPS = HEAD_STEPS + BODY_STEPS

            def attended(n, e0, bank_free, par, ts=slice(0, IT)):
                b0, k = 4 * par, ts.stop - ts.start
                num = psum[:, b0 + ts.start:b0 + ts.stop, 0:F]
                dps = psum[:, b0 + ts.start:b0 + ts.stop, F:FV]
                nc.vector.tensor_scalar(lone[:, ts, :], dps, 0.0, None, ALU.is_equal).then_inc(s_epi, 1)
                dve.wait_ge(s_epi, e0 + 1)
                nc.vector.tensor_tensor(den[:, ts, :], dps, lone[:, ts, :], ALU.add).then_inc(s_epi, 1)
                nc.vector.tensor_tensor(unif[:, ts, :], wh_mean[:, :, :].to_broadcast([P, k, F]),
                                        lone[:, ts, :].to_broadcast([P, k, F]), ALU.mult).then_inc(s_epi, 1)
                dve.wait_ge(s_epi, e0 + 3)
                nc.vector.reciprocal(rden[:, ts, :], den[:, ts, :]).then_inc(s_epi, 1)
                dve.wait_ge(s_epi, e0 + 4)
                nc.vector.tensor_tensor(agg[:, ts, :], num, rden[:, ts, :].to_broadcast([P, k, F]),
                                        ALU.mult).then_inc(s_bank[par], 1)
                dve.wait_ge(s_bank[par], bank_free)
                nc.vector.tensor_tensor(agg[:, ts, :], agg[:, ts, :], unif[:, ts, :], ALU.add).then_inc(s_epi, 1)
                dve.wait_ge(s_epi, e0 + 5)
                nc.vector.tensor_scalar(neg[:, ts, :], agg[:, ts, :], 0.0, None, ALU.min).then_inc(s_neg_h, 1)
                nc.vector.tensor_scalar(agg[:, ts, :], agg[:, ts, :], 0.0, -1.0, ALU.max, ALU.add).then_inc(s_epi, 1)
                dve.wait_ge(s_epi, e0 + 6)
                nc.vector.tensor_tensor(agg[:, ts, :], agg[:, ts, :], x_in[:, ts, :], ALU.add).then_inc(s_xused, 1)

            def residual(n, e0, ts=slice(0, IT)):
                dve.wait_ge(s_xused, n + 1)
                dve.wait_ge(s_exp, n + 1)
                nc.vector.tensor_tensor(res[:, ts, :], agg[:, ts, :], expd[:, ts, :], ALU.add).then_inc(s_epi, 1)
                dve.wait_ge(s_epi, e0 + 1)
                for t in range(ts.start, ts.stop):
                    op = nc.vector.bn_stats(stats[:, t, :], res[:, t, :])
                op.then_inc(s_epi, 1)
                dve.wait_ge(s_epi, e0 + 2)
                nc.vector.tensor_tensor(mdif[:, ts, :], stats[:, ts, 1:2], stats[:, ts, 4:5],
                                        ALU.subtract).then_inc(s_epi, 1)
                nc.vector.tensor_tensor(msum[:, ts, :], stats[:, ts, 1:2], stats[:, ts, 4:5],
                                        ALU.add).then_inc(s_epi, 1)
                nc.vector.tensor_tensor(vsum[:, ts, :], stats[:, ts, 2:3], stats[:, ts, 5:6],
                                        ALU.add).then_inc(s_epi, 1)
                dve.wait_ge(s_epi, e0 + 5)
                nc.vector.scalar_tensor_tensor(out=mdif[:, ts, :], in0=mdif[:, ts, :], scalar=F / 4,
                                               in1=mdif[:, ts, :], op0=ALU.mult, op1=ALU.mult).then_inc(s_epi, 1)
                nc.vector.tensor_scalar(mean[:, ts, :], msum[:, ts, :], 0.5, None, ALU.mult).then_inc(s_epi, 1)
                dve.wait_ge(s_epi, e0 + 7)
                nc.vector.tensor_tensor(vsum[:, ts, :], vsum[:, ts, :], mdif[:, ts, :], ALU.add).then_inc(s_var, 1)

            def normed(n, ts=slice(0, IT)):
                dve.wait_ge(s_sd, n + 1)
                nc.vector.reciprocal(rstd[:, ts, :], sdev[:, ts, :]).then_inc(s_rstd, 1)
                dve.wait_ge(s_rstd, n + 1)
                for t in range(ts.start, ts.stop):
                    op = nc.vector.tensor_scalar(y_out[:, t, :], res[:, t, :], mean[:, t, 0:1], rstd[:, t, 0:1],
                                                 ALU.subtract, ALU.mult)
                op.then_inc(s_y, 1)

            def group(g, before, half, par):
                dve.wait_ge(s_gamma, g * 16)
                weights(g, par, 0)
                dve.wait_ge(s_used, g * C + R)
                dve.wait_ge(s_xin, g * 16)
                attended(before, before * STEPS, half + 2, 1 - par)
                weights(g, par, 1)
                residual(before, before * STEPS + HEAD_STEPS)
                weights(g, par, 2)
                dve.wait_ge(s_yfree, g)
                normed(before)
                weights(g, par, 3)

            weights(0, 0, 0)
            dve.wait_ge(s_mean, 1)
            nc.vector.tensor_copy(wh_mean[:, 0, :], psum[:, 4, 0:F]).then_inc(s_bank[1], 1)
            for sweep in range(1, SW):
                weights(0, 0, sweep)
            with dve.Fori(0, G // 2 - 1) as m:
                group(m * 2 + 1, m * 2, m, 1)
                group(m * 2 + 2, m * 2 + 1, m, 0)
            group(G - 1, G - 2, G // 2 - 1, 1)
            halves = [slice(0, IT // 2), slice(IT // 2, IT)]
            e0 = (G - 1) * STEPS
            dve.wait_ge(s_xin, G * 16)
            dve.wait_ge(s_half, G)
            for k, ts in enumerate(halves):
                if k:
                    dve.wait_ge(s_used, G * C + R)
                attended(G - 1 + k, e0 + k * HEAD_STEPS, G // 2 + 1 + k, 1, ts)
            for k, ts in enumerate(halves):
                residual(G - 1 + k, e0 + 2 * HEAD_STEPS + k * BODY_STEPS, ts)
            dve.wait_ge(s_yfree, G)
            for k, ts in enumerate(halves):
                normed(G - 1 + k, ts)

        @block.tensor
        def _(pe):
            pe.wait_ge(s_small, 48)
            nc.tensor.matmul(psum[:, 4, 0:2], w_tr[:, :], a_sb[:, :], start=True, stop=True).then_inc(s_wa, 1)
            pe.wait_ge(s_wasb, 3)
            for b in range(JT // 4):
                if b % 2 == 0:
                    pe.wait_ge(s_xt[b // 2], 16)
                if b >= len(WH_BANKS):
                    last = b - len(WH_BANKS)
                    pe.wait_ge([s_wh_dve, s_wh_act][last % 2], last // 2 + 1)
                for q in range(4):
                    jt = 4 * b + q
                    op = nc.tensor.matmul(wh_banks(b)[:, q // HALF, (q % HALF) * FX:(q % HALF + 1) * FX],
                                          xt_flat[:, jt * P:(jt + 1) * P], w_ext[:, :], start=True, stop=True)
                op.then_inc(s_wh, 1)
            nc.tensor.matmul(psum[:, 7, :], wa1[:, :], xt_flat[:, 0:GW], start=True, stop=True).then_inc(s_s0, 1)
            pe.wait_ge(s_ident, 1)
            pe.wait_ge(s_tp, 1)
            nc.tensor.transpose(psum[0:1, 6, 0:P], tmax_p[:, :], ident[:, :]).then_inc(s_tpt, 1)
            pe.wait_ge(s_const, 2)
            pe.wait_ge(s_t1, 1)
            nc.tensor.matmul(psum[:, 4, 0:1], ones[:, :], tmax_1[:, :], start=True, stop=True).then_inc(s_tb, 1)
            pe.sem_inc(s_bank[0], 1)
            pe.wait_ge(s_clip, 2)
            nc.tensor.transpose(psum[0:JT, 6, 0:P], clip[:, :], ident[:, :]).then_inc(s_clip_t, 1)
            pe.wait_ge(s_xsum, 2)
            nc.tensor.matmul(psum[:, 4, 0:F], xmean[:, :], w_ext[:, 0:F], start=True, stop=True).then_inc(s_mean, 1)
            pe.sem_inc(s_used, R)

            def product(par, r, q, t, jt):
                return nc.tensor.matmul(psum[:, 4 * par + t, 0:FV], wgt_ring[:, r, q, t * P:(t + 1) * P],
                                        vals[:, jt, 0:FV], start=(jt == 0), stop=(jt == JT - 1))

            def products(g, par):
                for n in range(C - 1):
                    pe.wait_ge(s_wgt, g * C + (n + 1))
                    for q in range(CJ):
                        for t in range(IT):
                            op = product(par, n % R, q, t, n * CJ + q)
                    op.then_inc(s_used, 1)
                pe.wait_ge(s_wgt, g * C + C)
                for t in range(IT):
                    for q in range(CJ):
                        op = product(par, (C - 1) % R, q, t, (C - 1) * CJ + q)
                    if t == IT // 2 - 1:
                        op.then_inc(s_half, 1)
                op.then_inc(s_used, 1)

            with pe.Fori(0, G // 2) as m:
                for par in range(2):
                    pe.wait_ge(s_bank[par], m + 1)
                    products(m * 2 + par, par)


def kernel(x, adj, L0_gnn_W, L0_gnn_a):
    import numpy as np
    import concourse.bacc as bacc
    from concourse.bass_utils import run_bass_kernel_spmd

    x = np.ascontiguousarray(x)
    adj = np.asarray(adj)
    w = np.ascontiguousarray(L0_gnn_W)
    n = x.shape[0]
    rows, tiles = 512, 4
    adj_t = adj.reshape(n // rows, rows, n // (tiles * 128), tiles, 128).transpose(0, 2, 4, 3, 1)
    arrays = {
        "adj_t": np.ascontiguousarray(adj_t).reshape(-1, 128, tiles * rows),
        "x_t": np.ascontiguousarray(x.T),
        "x": x,
        "w": w,
        "w_t": np.ascontiguousarray(w.T),
        "a_t": np.ascontiguousarray(np.asarray(L0_gnn_a).reshape(2, -1).T),
    }
    nc = bacc.Bacc("TRN2", target_bir_lowering=False, num_devices=1)
    args = [nc.dram_tensor(k, v.shape, mybir.dt.from_np(v.dtype), kind="ExternalInput").ap()
            for k, v in arrays.items()]
    out = nc.dram_tensor("out", x.shape, F32, kind="ExternalOutput").ap()
    gat_norm(nc, *args, out)
    r = run_bass_kernel_spmd(nc, [arrays], core_ids=[0])
    return r.results[0]["out"]
```

```python
import math
from contextlib import ExitStack

import concourse.bass as bass
from concourse import mybir

ALU = mybir.AluOpType
ACT = mybir.ActivationFunctionType
AX = mybir.AxisListType
F32 = mybir.dt.float32
BF16 = mybir.dt.bfloat16
I32 = mybir.dt.int32
RMAX = bass.bass_isa.ReduceOp.max

P = 128
ALPHA = 0.2
EPS = 1e-05


def gat_norm(nc, adj_t, x_t, x, w, w_t, a_t, out):
    N, F = x.shape
    JT = N // P
    IT = 4
    SPREAD = 80.0
    FAR = 1e30
    TINY = 1e-37
    GW = IT * P
    G = N // GW
    CJ = adj_t.shape[2] // GW
    C = JT // CJ
    R = 4
    SW = C // R
    FV = F + 1
    FX = F + 2
    XD = 8
    XA = 2
    FOLDS = [512, 256, 128]
    WH_BANKS = [0, 2, 5]
    LATE = 2
    HALF = 2

    with ExitStack() as ctx:
        def sb(name, shape, dt=F32):
            return ctx.enter_context(nc.sbuf_tensor(name, shape, dt))

        def sem(name):
            return ctx.enter_context(nc.semaphore(name))

        adj_ring = sb("adj_ring", [P, R, CJ, GW], I32)
        edge_ring = sb("edge_ring", [P, R, CJ, GW], BF16)
        wgt_ring = sb("wgt_ring", [P, R, CJ, GW])
        gamma = sb("gamma", [P, 2, GW])
        gamma_rows = sb("gamma_rows", [JT, P])
        vals = sb("vals", [P, JT, FX])
        beta = sb("beta", [P, JT])
        clip = sb("clip", [P, JT])
        w_ext = sb("w_ext", [P, FX])
        w_tr = sb("w_tr", [P, F])
        a_sb = sb("a_sb", [P, 2])
        wa1 = sb("wa1", [P, P])
        ident = sb("ident", [P, P])
        ones = sb("ones", [1, P])
        low = sb("low", [P, JT])
        low_p = sb("low_p", [P, 1])
        low_all = sb("low_all", [P, 1])
        wide = sb("wide", [1, 1], I32)
        tmax_p = sb("tmax_p", [P, 1])
        tmax_1 = sb("tmax_1", [1, 1])
        tmax = sb("tmax", [P, 3])
        eps_sb = sb("eps_sb", [P, 1])
        xfold = sb("xfold", [P, XA + N // XD])
        xsum = sb("xsum", [P, 1])
        xmean = sb("xmean", [P, P])
        wh_mean = sb("wh_mean", [P, 1, F])
        x_in = sb("x_in", [P, IT, F])
        lone = sb("lone", [P, IT, 1])
        den = sb("den", [P, IT, 1])
        rden = sb("rden", [P, IT, 1])
        agg = sb("agg", [P, IT, F])
        unif = sb("unif", [P, IT, F])
        neg = sb("neg", [P, IT, F])
        expd = sb("expd", [P, IT, F])
        res = sb("res", [P, IT, F])
        stats = sb("stats", [P, IT, 6])
        mdif = sb("mdif", [P, IT, 1])
        msum = sb("msum", [P, IT, 1])
        vsum = sb("vsum", [P, IT, 1])
        mean = sb("mean", [P, IT, 1])
        sdev = sb("sdev", [P, IT, 1])
        rstd = sb("rstd", [P, IT, 1])
        y_out = sb("y_out", [P, IT, F])
        psum = ctx.enter_context(nc.psum_tensor("psum", [P, 8, GW], F32))
        gamma_dram = nc.dram_tensor("gamma_dram", [JT, P], F32, kind="Internal").ap()
        gamma_groups = gamma_dram.rearrange("(g t) p -> g (t p)", t=IT)

        xt_flat = wgt_ring[:, :, :, :].rearrange("p r q i -> p (r q i)")
        XC = N // XD
        SLOT = CJ * GW

        s_small = sem("s_small")
        s_xt = [sem(f"s_xt{r}") for r in range(XD)]
        s_adj = [sem(f"s_adj{r}") for r in range(R)]
        s_const = sem("s_const")
        s_id0 = sem("s_id0")
        s_ident = sem("s_ident")
        s_wa = sem("s_wa")
        s_wasb = sem("s_wasb")
        s_wh = sem("s_wh")
        s_wh_dve = sem("s_wh_dve")
        s_wh_act = sem("s_wh_act")
        s_s0 = sem("s_s0")
        s_clip = sem("s_clip")
        s_clip_t = sem("s_clip_t")
        s_gamma0 = sem("s_gamma0")
        s_gamma_row = sem("s_gamma_row")
        s_gamma_st = sem("s_gamma_st")
        s_gamma = sem("s_gamma")
        s_tp = sem("s_tp")
        s_tpt = sem("s_tpt")
        s_t1 = sem("s_t1")
        s_tb = sem("s_tb")
        s_tmax = sem("s_tmax")
        s_beta = sem("s_beta")
        s_vals = sem("s_vals")
        s_xs = sem("s_xs")
        s_xs_act = sem("s_xs_act")
        s_xsum = sem("s_xsum")
        s_mean = sem("s_mean")
        s_edge = sem("s_edge")
        s_wgt = sem("s_wgt")
        s_used = sem("s_used")
        s_bank = [sem(f"s_bank{p}") for p in range(2)]
        s_epi = sem("s_epi")
        s_neg_h = sem("s_neg_h")
        s_exp = sem("s_exp")
        s_var = sem("s_var")
        s_sd = sem("s_sd")
        s_rstd = sem("s_rstd")
        s_xin = sem("s_xin")
        s_xused = sem("s_xused")
        s_y = sem("s_y")
        s_out = sem("s_out")
        s_last = [sem(f"s_last{k}") for k in range(2)]
        s_half = sem("s_half")
        s_yfree = sem("s_yfree")

        s_narrow = sem("s_narrow")
        s_flag = sem("s_flag")
        c_xt = sem("c_xt")
        c_wh = sem("c_wh")
        c_whsb = sem("c_whsb")
        c_set = sem("c_set")
        c_xg = sem("c_xg")
        c_s = sem("c_s")
        c_ssb = sem("c_ssb")
        c_adj = sem("c_adj")
        c_seen = sem("c_seen")
        c_max = sem("c_max")
        c_mx = sem("c_mx")
        c_row = sem("c_row")
        c_m = sem("c_m")
        c_e = sem("c_e")
        c_d = sem("c_d")
        c_p = sem("c_p")
        c_w = sem("c_w")
        c_mm = sem("c_mm")
        c_acc = sem("c_acc")
        c_xin = sem("c_xin")
        c_out = sem("c_out")
        c_passed = sem("c_passed")

        c_sums = xt_flat[:, 0:IT * FV].rearrange("p (t f) -> p t f", t=IT)
        c_xtile = wgt_ring[:, 0, 2, 0:P]
        c_z, c_leaky, c_diff, c_prob = (wgt_ring[:, 1, q, :] for q in range(4))
        c_wgt, c_high, c_rowmax, c_sub = (wgt_ring[:, 2, q, :] for q in range(4))
        c_srow, c_xcols, c_edge, c_tedge = (wgt_ring[:, 3, q, :] for q in range(4))
        t_col = beta

        x_rows = x.rearrange("(g t p) f -> g p t f", t=IT, p=P)
        out_rows = out.rearrange("(g t p) f -> g p t f", t=IT, p=P)

        def wh_banks(b):
            first = WH_BANKS[b % len(WH_BANKS)]
            return psum[:, first:first + 2, 0:HALF * FX]

        block = ctx.enter_context(nc.Block())

        @block.sync
        def _(sp):
            sp.dma_start(w_tr[:, :], w_t).then_inc(s_small, 16)
            sp.dma_start(a_sb[:, :], a_t).then_inc(s_small, 16)
            sp.dma_start(w_ext[:, 0:F], w).then_inc(s_small, 16)
            for r in range(XD):
                sp.dma_start(xt_flat[:, r * XC:(r + 1) * XC], x_t[:, r * XC:(r + 1) * XC]).then_inc(s_xt[r], 16)
            for r in range(R):
                sp.dma_start(adj_ring[:, r].rearrange("p q i -> p (q i)"), adj_t[r]).then_inc(s_adj[r], 16)
            with sp.Fori(1, G * SW) as k:
                for r in range(R):
                    sp.wait_ge(s_edge, k * R + (r + 1 - R))
                    sp.dma_start(adj_ring[:, r].rearrange("p q i -> p (q i)"),
                                 adj_t[bass.ds(k * R + r, 1)].rearrange("o p n -> (o p) n")).then_inc(s_adj[r], 16)

            sp.wait_ge(s_flag, 1)
            with sp.If(sp.value_load(wide[0:1, 0:1]) > 0):
                sp.wait_ge(s_y, G + 1)
                sp.wait_ge(s_out, 16 * (G - 1))
                sp.wait_ge(s_last[0], 16)
                sp.wait_ge(s_last[1], 16)
                sp.dma_start(c_xtile, x_t[:, 0:P]).then_inc(c_xt, 16)
                with sp.Fori(1, JT) as jt:
                    sp.wait_ge(c_wh, jt)
                    sp.dma_start(c_xtile, x_t[:, bass.ds(jt * P, P)]).then_inc(c_xt, 16)
                sp.wait_ge(c_whsb, JT)
                with sp.Fori(0, G) as g:
                    sp.dma_start(c_xcols, x_t[:, bass.ds(g * GW, GW)]).then_inc(c_xg, 16)
                    sp.dma_start(x_in[:, :, :], x_rows[bass.ds(g, 1)].rearrange("o p t f -> (o p) t f")
                                 ).then_inc(c_xin, 16)
                    for sweep in range(2):
                        with sp.Fori(0, C) as c:
                            sp.dma_start(adj_ring[:, 0].rearrange("p q i -> p (q i)"),
                                         adj_t[bass.ds(g * C + c, 1)].rearrange("o p n -> (o p) n")).then_inc(c_adj, 16)
                            sp.wait_ge(c_seen, (g * 2 + sweep) * C + c + 1)
                            sp.sem_inc(c_passed, 1)
                    sp.wait_ge(s_y, g + (G + 2))
                    sp.dma_start(out_rows[bass.ds(g, 1)].rearrange("o p t f -> (o p) t f"), y_out[:, :, :]
                                 ).then_inc(c_out, 16)
                    sp.wait_ge(c_out, g * 16 + 16)
                    sp.sem_inc(c_passed, 1)

        @block.gpsimd
        def _(pool):
            nc.gpsimd.memset(ident[:, :], 0.0).then_inc(s_id0, 1)
            pool.wait_ge(s_id0, 1)
            nc.gpsimd.affine_select(out=ident[:, :], in_=ident[:, :], compare_op=ALU.not_equal, fill=1.0, base=0,
                                    pattern=[[-1, P]], channel_multiplier=1).then_inc(s_ident, 1)
            pool.sem_inc(s_yfree, 1)
            fold = xfold[:, XA:XA + XC]
            pool.wait_ge(s_xt[XA], 16)
            pool.wait_ge(s_xt[XA + 1], 16)
            nc.gpsimd.tensor_tensor(fold, xt_flat[:, XA * XC:(XA + 1) * XC], xt_flat[:, (XA + 1) * XC:(XA + 2) * XC],
                                    ALU.add).then_inc(s_xs, 1)
            for k in range(XA + 2, XD):
                pool.wait_ge(s_xt[k], 16)
                pool.wait_ge(s_xs, k - XA - 1)
                nc.gpsimd.tensor_tensor(fold, fold, xt_flat[:, k * XC:(k + 1) * XC], ALU.add).then_inc(s_xs, 1)
            for k, half in enumerate(FOLDS):
                pool.wait_ge(s_xs, XD - XA - 1 + k)
                nc.gpsimd.tensor_tensor(fold[:, 0:half], fold[:, 0:half], fold[:, half:2 * half],
                                        ALU.add).then_inc(s_xs, 1)
            pool.dma_start(x_in[:, :, :], x_rows[0]).then_inc(s_xin, 16)
            pool.wait_ge(s_gamma_row, 1)
            pool.dma_start(gamma_dram, gamma_rows[:, :]).then_inc(s_gamma_st, 16)
            pool.wait_ge(s_gamma_st, 16)
            pool.dma_start(gamma[:, 1, :], gamma_groups[1].partition_broadcast(P)).then_inc(s_gamma, 16)

            pool.wait_ge(s_narrow, 2)
            nc.gpsimd.partition_all_reduce(low_all[:, :], low_p[:, :], P, RMAX).then_inc(s_narrow, 1)

            def load_x(g):
                pool.wait_ge(s_xused, g)
                rows = x_rows[g] if isinstance(g, int) else x_rows[bass.ds(g, 1)].rearrange("o p t f -> (o p) t f")
                pool.dma_start(x_in[:, :, :], rows).then_inc(s_xin, 16)

            def stored(g):
                pool.wait_ge(s_out, g * 16 + 16)
                pool.sem_inc(s_yfree, 1)

            with pool.Fori(0, G // 2 - 1) as m:
                for par in range(2):
                    load_x(m * 2 + (par + 1))
                    pool.dma_start(gamma[:, par, :], gamma_groups[bass.ds(m * 2 + (par + 2), 1)].rearrange(
                        "o n -> (o n)").partition_broadcast(P)).then_inc(s_gamma, 16)
                    stored(m * 2 + par)
            load_x(G - 1)
            stored(G - 2)
            pool.wait_ge(s_flag, 1)
            with pool.If(pool.value_load(wide[0:1, 0:1]) > 0):
                with pool.Fori(0, G) as g:
                    pool.wait_ge(c_mx, g + 1)
                    pool.sem_inc(c_passed, 1)
                    nc.gpsimd.partition_all_reduce(c_rowmax, c_high, P, RMAX).then_inc(c_row, 1)

        @block.scalar
        def _(act):
            def edges(c, r, first=False):
                act.wait_ge(s_adj[r], c * 16 + 16)
                if not first:
                    act.wait_ge(s_wgt, c * R + (r + 1 - R))
                nc.scalar.activation(edge_ring[:, r].rearrange("p q i -> p (q i)"),
                                     adj_ring[:, r].rearrange("p q i -> p (q i)"), ACT.Relu).then_inc(s_edge, 1)

            for b in range(1, JT // 4, 2):
                act.wait_ge(s_wh, b + 1)
                nc.scalar.copy(vals[:, 4 * b:4 * b + 4, :].rearrange("p (k h) f -> p k (h f)", h=HALF),
                               wh_banks(b)).then_inc(s_wh_act, 1)
                if b // 2 < XA:
                    act.wait_ge(s_xt[b // 2], 16)
                    nc.scalar.activation(edge_ring[:, R - 1 - b // 2].rearrange("p q i -> p (q i)")[:, 0:XC],
                                         xt_flat[:, b // 2 * XC:(b // 2 + 1) * XC], ACT.Copy,
                                         accum_out=xfold[:, b // 2:b // 2 + 1]).then_inc(s_xs_act, 1)
            edges(0, 0, True)
            act.wait_ge(s_tmax, 3)
            nc.scalar.activation(beta[:, :], vals[:, :, F], ACT.Exp, bias=tmax[:, 1:2],
                                 scale=1 - ALPHA).then_inc(s_beta, 1)
            act.wait_ge(s_beta, 1)
            nc.scalar.activation(vals[:, :, F], vals[:, :, F], ACT.Exp, bias=tmax[:, 2:3],
                                 scale=ALPHA).then_inc(s_beta, 1)
            act.wait_ge(s_clip, 1)
            nc.scalar.activation(gamma[:, 0, :], gamma[:, 0, :], ACT.Exp, scale=-(1 - ALPHA)).then_inc(s_gamma0, 1)
            act.wait_ge(s_clip_t, 1)
            nc.scalar.activation(gamma_rows[:, :], psum[0:JT, 6, 0:P], ACT.Exp,
                                 scale=-(1 - ALPHA)).then_inc(s_gamma_row, 1)
            act.wait_ge(s_xs_act, XA)
            for r in range(1, R):
                edges(0, r, True)
            with act.Fori(1, SW) as k:
                for r in range(R):
                    edges(k, r)

            def exp_h(n, ts=slice(0, IT)):
                act.wait_ge(s_neg_h, n + 1)
                nc.scalar.activation(expd[:, ts, :], neg[:, ts, :], ACT.Exp).then_inc(s_exp, 1)

            def sqrt_var(n, ts=slice(0, IT)):
                act.wait_ge(s_var, n + 1)
                nc.scalar.activation(sdev[:, ts, :], vsum[:, ts, :], ACT.Sqrt, bias=eps_sb[:, :],
                                     scale=1.0 / F).then_inc(s_sd, 1)

            with act.Fori(0, G - 1) as g:
                for sweep in range(SW):
                    for r in range(R):
                        edges((g + 1) * SW + sweep, r)
                    if sweep == 0:
                        exp_h(g)
                    if sweep == 1:
                        sqrt_var(g)
                act.wait_ge(s_y, g + 1)
                act.dma_start(out_rows[bass.ds(g, 1)].rearrange("o p t f -> (o p) t f"), y_out[:, :, :]
                              ).then_inc(s_out, 16)
            halves = [slice(0, IT // 2), slice(IT // 2, IT)]
            for k, ts in enumerate(halves):
                exp_h(G - 1 + k, ts)
            for k, ts in enumerate(halves):
                sqrt_var(G - 1 + k, ts)
            for k, ts in enumerate(halves):
                act.wait_ge(s_y, G + k)
                act.dma_start(out_rows[G - 1][:, ts, :], y_out[:, ts, :]).then_inc(s_last[k], 16)
            act.wait_ge(s_out, 16 * (G - 1))
            act.wait_ge(s_last[0], 16)
            act.wait_ge(s_last[1], 16)
            act.wait_ge(s_flag, 1)
            with act.If(act.value_load(wide[0:1, 0:1]) > 0):
                with act.Fori(0, G) as g:
                    with act.Fori(0, JT) as jt:
                        act.wait_ge(c_d, g * JT + jt + 1)
                        nc.scalar.activation(c_prob, c_diff, ACT.Exp).then_inc(c_p, 1)
                    exp_h(g + (G + 1))
                    sqrt_var(g + (G + 1))

        @block.vector
        def _(dve):
            nc.vector.memset(eps_sb[:, :], EPS).then_inc(s_const, 1)
            nc.vector.memset(ones[:, :], 1.0).then_inc(s_const, 1)
            dve.wait_ge(s_wa, 1)
            nc.vector.tensor_copy(w_ext[:, F:F + 1], psum[:, 4, 1:2]).then_inc(s_wasb, 1)
            nc.vector.tensor_copy(w_ext[:, F + 1:FX], psum[:, 4, 0:1]).then_inc(s_wasb, 1)
            nc.vector.tensor_copy(wa1[:, :], psum[:, 4, 0:1].to_broadcast([P, P])).then_inc(s_wasb, 1)
            for b in range(0, JT // 4, 2):
                dve.wait_ge(s_wh, b + 1)
                nc.vector.tensor_copy(vals[:, 4 * b:4 * b + 4, :].rearrange("p (k h) f -> p k (h f)", h=HALF),
                                      wh_banks(b)).then_inc(s_wh_dve, 1)
            dve.wait_ge(s_wh_dve, JT // 8)
            dve.wait_ge(s_wh_act, JT // 8)
            nc.vector.tensor_reduce(tmax_p[:, :], vals[:, :, F], AX.X, ALU.max).then_inc(s_tp, 1)
            dve.wait_ge(s_tpt, 1)
            nc.vector.tensor_reduce(tmax_1[:, :], psum[0:1, 6, 0:P], AX.X, ALU.max).then_inc(s_t1, 1)
            dve.wait_ge(s_tb, 1)
            nc.vector.tensor_scalar(tmax[:, 1:2], psum[:, 4, 0:1], -(1 - ALPHA), None, ALU.mult).then_inc(s_tmax, 1)
            nc.vector.tensor_scalar(tmax[:, 2:3], psum[:, 4, 0:1], -ALPHA, None, ALU.mult).then_inc(s_tmax, 1)
            nc.vector.tensor_copy(tmax[:, 0:1], psum[:, 4, 0:1]).then_inc(s_tmax, 1)
            dve.wait_ge(s_tmax, 3)
            dve.wait_ge(s_s0, 1)
            nc.vector.tensor_scalar(gamma[:, 0, :], psum[:, 7, :], tmax[:, 0:1], 0.0,
                                    ALU.add, ALU.max).then_inc(s_clip, 1)
            nc.vector.tensor_scalar(clip[:, :], vals[:, :, F + 1], tmax[:, 0:1], 0.0,
                                    ALU.add, ALU.max).then_inc(s_clip, 1)
            dve.wait_ge(s_xs_act, XA)
            dve.wait_ge(s_xs, XD - XA - 1 + len(FOLDS))
            nc.vector.tensor_reduce(xsum[:, :], xfold[:, 0:XA + FOLDS[-1]], AX.X, ALU.add).then_inc(s_xsum, 1)
            dve.wait_ge(s_xsum, 1)
            nc.vector.tensor_scalar(xmean[:, :], xsum[:, 0:1].to_broadcast([P, P]), 1.0 / N, None,
                                    ALU.mult).then_inc(s_xsum, 1)
            dve.wait_ge(s_beta, 2)

            def weights(g, par, sweep):
                for r in range(R):
                    c = g * C + sweep * R + r
                    if isinstance(g, int) and g == 0:
                        jts = slice((sweep * R + r) * CJ, (sweep * R + r + 1) * CJ)
                        nc.vector.tensor_tensor(vals[:, jts, 0:F], vals[:, jts, 0:F],
                                                vals[:, jts, F:F + 1].to_broadcast([P, CJ, F]),
                                                ALU.mult).then_inc(s_vals, 1)
                        dve.wait_ge(s_gamma0, 1)
                    dve.wait_ge(s_edge, c + 1)
                    dve.wait_ge(s_used, c + 1)
                    for q in range(CJ):
                        jt = (sweep * R + r) * CJ + q
                        op = nc.vector.scalar_tensor_tensor(
                            out=wgt_ring[:, r, q, :], in0=gamma[:, par, :], scalar=beta[:, jt:jt + 1],
                            in1=edge_ring[:, r, q, :], op0=ALU.max, op1=ALU.min)
                    op.then_inc(s_wgt, 1)

            HEAD_STEPS, BODY_STEPS = 6, 7
            STEPS = HEAD_STEPS + BODY_STEPS

            def attended(e0, bank_free, par, ts=slice(0, IT), sums=None):
                k = ts.stop - ts.start
                if sums is None:
                    sums = psum[:, 4 * par:4 * par + IT, :]
                num, dps = sums[:, ts, 0:F], sums[:, ts, F:FV]
                nc.vector.tensor_scalar(lone[:, ts, :], dps, 0.0, None, ALU.is_equal).then_inc(s_epi, 1)
                dve.wait_ge(s_epi, e0 + 1)
                nc.vector.scalar_tensor_tensor(out=den[:, ts, :], in0=dps, scalar=TINY, in1=lone[:, ts, :],
                                               op0=ALU.max, op1=ALU.add).then_inc(s_epi, 1)
                nc.vector.tensor_tensor(unif[:, ts, :], wh_mean[:, :, :].to_broadcast([P, k, F]),
                                        lone[:, ts, :].to_broadcast([P, k, F]), ALU.mult).then_inc(s_epi, 1)
                dve.wait_ge(s_epi, e0 + 3)
                nc.vector.reciprocal(rden[:, ts, :], den[:, ts, :]).then_inc(s_epi, 1)
                dve.wait_ge(s_epi, e0 + 4)
                nc.vector.tensor_tensor(agg[:, ts, :], num, rden[:, ts, :].to_broadcast([P, k, F]),
                                        ALU.mult).then_inc(s_bank[par], 1)
                dve.wait_ge(s_bank[par], bank_free)
                nc.vector.tensor_tensor(agg[:, ts, :], agg[:, ts, :], unif[:, ts, :], ALU.add).then_inc(s_epi, 1)
                dve.wait_ge(s_epi, e0 + 5)
                nc.vector.tensor_scalar(neg[:, ts, :], agg[:, ts, :], 0.0, None, ALU.min).then_inc(s_neg_h, 1)
                nc.vector.tensor_scalar(agg[:, ts, :], agg[:, ts, :], 0.0, -1.0, ALU.max, ALU.add).then_inc(s_epi, 1)
                dve.wait_ge(s_epi, e0 + 6)
                nc.vector.tensor_tensor(agg[:, ts, :], agg[:, ts, :], x_in[:, ts, :], ALU.add).then_inc(s_xused, 1)

            def residual(n, e0, ts=slice(0, IT)):
                dve.wait_ge(s_xused, n + 1)
                dve.wait_ge(s_exp, n + 1)
                nc.vector.tensor_tensor(res[:, ts, :], agg[:, ts, :], expd[:, ts, :], ALU.add).then_inc(s_epi, 1)
                dve.wait_ge(s_epi, e0 + 1)
                for t in range(ts.start, ts.stop):
                    op = nc.vector.bn_stats(stats[:, t, :], res[:, t, :])
                op.then_inc(s_epi, 1)
                dve.wait_ge(s_epi, e0 + 2)
                nc.vector.tensor_tensor(mdif[:, ts, :], stats[:, ts, 1:2], stats[:, ts, 4:5],
                                        ALU.subtract).then_inc(s_epi, 1)
                nc.vector.tensor_tensor(msum[:, ts, :], stats[:, ts, 1:2], stats[:, ts, 4:5],
                                        ALU.add).then_inc(s_epi, 1)
                nc.vector.tensor_tensor(vsum[:, ts, :], stats[:, ts, 2:3], stats[:, ts, 5:6],
                                        ALU.add).then_inc(s_epi, 1)
                dve.wait_ge(s_epi, e0 + 5)
                nc.vector.scalar_tensor_tensor(out=mdif[:, ts, :], in0=mdif[:, ts, :], scalar=F / 4,
                                               in1=mdif[:, ts, :], op0=ALU.mult, op1=ALU.mult).then_inc(s_epi, 1)
                nc.vector.tensor_scalar(mean[:, ts, :], msum[:, ts, :], 0.5, None, ALU.mult).then_inc(s_epi, 1)
                dve.wait_ge(s_epi, e0 + 7)
                nc.vector.tensor_tensor(vsum[:, ts, :], vsum[:, ts, :], mdif[:, ts, :], ALU.add).then_inc(s_var, 1)

            def normed(n, ts=slice(0, IT)):
                dve.wait_ge(s_sd, n + 1)
                nc.vector.reciprocal(rstd[:, ts, :], sdev[:, ts, :]).then_inc(s_rstd, 1)
                dve.wait_ge(s_rstd, n + 1)
                for t in range(ts.start, ts.stop):
                    op = nc.vector.tensor_scalar(y_out[:, t, :], res[:, t, :], mean[:, t, 0:1], rstd[:, t, 0:1],
                                                 ALU.subtract, ALU.mult)
                op.then_inc(s_y, 1)

            def group(g, before, half, par):
                dve.wait_ge(s_gamma, g * 16)
                weights(g, par, 0)
                dve.wait_ge(s_used, g * C + R)
                dve.wait_ge(s_xin, g * 16)
                attended(before * STEPS, half + 2, 1 - par)
                weights(g, par, 1)
                residual(before, before * STEPS + HEAD_STEPS)
                weights(g, par, 2)
                dve.wait_ge(s_yfree, g)
                normed(before)
                weights(g, par, 3)

            weights(0, 0, 0)
            dve.wait_ge(s_mean, 1)
            nc.vector.tensor_copy(wh_mean[:, 0, :], psum[:, 4, 0:F]).then_inc(s_bank[1], 1)
            nc.vector.tensor_scalar(low[:, :], beta[:, :], math.exp(-(1 - ALPHA) * SPREAD), None,
                                    ALU.is_lt).then_inc(s_narrow, 1)
            dve.wait_ge(s_narrow, 1)
            nc.vector.tensor_reduce(low_p[:, :], low[:, :], AX.X, ALU.max).then_inc(s_narrow, 1)
            for sweep in range(1, SW - 1):
                weights(0, 0, sweep)
            dve.wait_ge(s_narrow, 3)
            nc.vector.tensor_copy(wide[:, :], low_all[0:1, :]).then_inc(s_flag, 1)
            weights(0, 0, SW - 1)
            with dve.Fori(0, G // 2 - 1) as m:
                group(m * 2 + 1, m * 2, m, 1)
                group(m * 2 + 2, m * 2 + 1, m, 0)
            group(G - 1, G - 2, G // 2 - 1, 1)
            halves = [slice(0, IT // 2), slice(IT // 2, IT)]
            e0 = (G - 1) * STEPS
            dve.wait_ge(s_xin, G * 16)
            dve.wait_ge(s_half, G)
            for k, ts in enumerate(halves):
                if k:
                    dve.wait_ge(s_used, G * C + R)
                attended(e0 + k * STEPS, G // 2 + 1 + k, 1, ts)
                residual(G - 1 + k, e0 + k * STEPS + HEAD_STEPS, ts)
            dve.wait_ge(s_yfree, G)
            for k, ts in enumerate(halves):
                normed(G - 1 + k, ts)

            dve.wait_ge(s_flag, 1)
            with dve.If(dve.value_load(wide[0:1, 0:1]) > 0):
                with dve.Fori(0, JT) as jt:
                    dve.wait_ge(c_wh, jt + 1)
                    nc.vector.tensor_copy(vals[:, bass.ds(jt, 1), :].rearrange("p o f -> p (o f)"),
                                          psum[:, 0, 0:FX]).then_inc(c_whsb, 1)
                dve.wait_ge(c_whsb, JT)
                nc.vector.tensor_copy(t_col[:, :], vals[:, :, F]).then_inc(c_set, 1)
                dve.wait_ge(c_set, 1)
                nc.vector.memset(vals[:, :, F:FV], 1.0).then_inc(c_set, 1)
                with dve.Fori(0, G) as g:
                    dve.wait_ge(c_s, g + 1)
                    nc.vector.memset(c_high, -FAR)
                    nc.vector.memset(c_sums, 0.0)
                    nc.vector.tensor_copy(c_srow, psum[:, 4, :]).then_inc(c_ssb, 1)
                    dve.wait_ge(c_ssb, g + 1)
                    dve.sem_inc(c_passed, 1)
                    with dve.Fori(0, C) as c:
                        dve.wait_ge(c_adj, ((g * 2) * C + c) * 16 + 16)
                        for q in range(CJ):
                            k0 = ((g * C + c) * CJ + q) * 3
                            nc.vector.tensor_scalar(c_edge, adj_ring[:, 0, q, :], 0.0, 2 * FAR, ALU.is_gt,
                                                    ALU.mult).then_inc(c_max, 1)
                            dve.wait_ge(c_max, k0 + 1)
                            nc.vector.tensor_scalar(c_tedge, c_edge, -FAR, t_col[:, bass.ds(c * CJ + q, 1)], ALU.add,
                                                    ALU.min).then_inc(c_max, 1)
                            dve.wait_ge(c_max, k0 + 2)
                            op = nc.vector.tensor_tensor(c_high, c_high, c_tedge, ALU.max)
                            if q == CJ - 1:
                                op.then_inc(c_seen, 1)
                                dve.sem_inc(c_max, 1)
                                dve.wait_ge(c_seen, (g * 2) * C + c + 1)
                            else:
                                op.then_inc(c_max, 1)
                                dve.wait_ge(c_max, k0 + 3)
                    nc.vector.tensor_copy(c_z, c_high).then_inc(c_mx, 1)
                    dve.wait_ge(c_row, g + 1)
                    nc.vector.tensor_tensor(c_z, c_srow, c_rowmax, ALU.add).then_inc(c_m, 1)
                    dve.wait_ge(c_m, g * 2 + 1)
                    nc.vector.scalar_tensor_tensor(out=c_sub, in0=c_z, scalar=ALPHA, in1=c_z, op0=ALU.mult,
                                                   op1=ALU.max).then_inc(c_m, 1)
                    dve.wait_ge(c_m, g * 2 + 2)
                    dve.sem_inc(c_passed, 1)
                    with dve.Fori(0, C) as c:
                        dve.wait_ge(c_adj, ((g * 2 + 1) * C + c) * 16 + 16)
                        for q in range(CJ):
                            k = (g * C + c) * CJ + q
                            nc.vector.tensor_scalar(c_z, c_srow, t_col[:, bass.ds(c * CJ + q, 1)], None,
                                                    ALU.add).then_inc(c_e, 1)
                            dve.wait_ge(c_e, k * 3 + 1)
                            nc.vector.scalar_tensor_tensor(out=c_leaky, in0=c_z, scalar=ALPHA, in1=c_z, op0=ALU.mult,
                                                           op1=ALU.max).then_inc(c_e, 1)
                            dve.wait_ge(c_e, k * 3 + 2)
                            nc.vector.tensor_tensor(c_tedge, c_leaky, c_sub, ALU.subtract).then_inc(c_e, 1)
                            dve.wait_ge(c_e, k * 3 + 3)
                            nc.vector.tensor_scalar(c_diff, c_tedge, 0.0, None, ALU.min).then_inc(c_d, 1)
                            dve.wait_ge(c_p, k + 1)
                            nc.vector.scalar_tensor_tensor(out=c_wgt, in0=adj_ring[:, 0, q, :], scalar=0.0, in1=c_prob,
                                                           op0=ALU.is_gt, op1=ALU.mult).then_inc(c_w, 1)
                            dve.wait_ge(c_mm, k + 1)
                            op = nc.vector.tensor_tensor(c_sums, c_sums, psum[:, 0:IT, 0:FV], ALU.add)
                            op.then_inc(c_acc, 1)
                            dve.wait_ge(c_acc, k + 1)
                        dve.sem_inc(c_seen, 1)
                    dve.wait_ge(c_xin, g * 16 + 16)
                    attended((g + (G + 1)) * STEPS, g + (G // 2 + 3), 1, sums=c_sums)
                    residual(g + (G + 1), (g + (G + 1)) * STEPS + HEAD_STEPS)
                    normed(g + (G + 1))

        @block.tensor
        def _(pe):
            pe.wait_ge(s_small, 48)
            nc.tensor.matmul(psum[:, 4, 0:2], w_tr[:, :], a_sb[:, :], start=True, stop=True).then_inc(s_wa, 1)
            pe.wait_ge(s_wasb, 3)
            for b in range(JT // 4):
                if b % 2 == 0:
                    pe.wait_ge(s_xt[b // 2], 16)
                if b >= len(WH_BANKS):
                    last = b - len(WH_BANKS)
                    pe.wait_ge([s_wh_dve, s_wh_act][last % 2], last // 2 + 1)
                for q in range(4):
                    jt = 4 * b + q
                    op = nc.tensor.matmul(wh_banks(b)[:, q // HALF, (q % HALF) * FX:(q % HALF + 1) * FX],
                                          xt_flat[:, jt * P:(jt + 1) * P], w_ext[:, :], start=True, stop=True)
                op.then_inc(s_wh, 1)
            nc.tensor.matmul(psum[:, 7, :], wa1[:, :], xt_flat[:, 0:GW], start=True, stop=True).then_inc(s_s0, 1)
            pe.wait_ge(s_ident, 1)
            pe.wait_ge(s_tp, 1)
            nc.tensor.transpose(psum[0:1, 6, 0:P], tmax_p[:, :], ident[:, :]).then_inc(s_tpt, 1)
            pe.wait_ge(s_const, 2)
            pe.wait_ge(s_t1, 1)
            nc.tensor.matmul(psum[:, 4, 0:1], ones[:, :], tmax_1[:, :], start=True, stop=True).then_inc(s_tb, 1)
            pe.sem_inc(s_bank[0], 1)
            pe.wait_ge(s_clip, 2)
            nc.tensor.transpose(psum[0:JT, 6, 0:P], clip[:, :], ident[:, :]).then_inc(s_clip_t, 1)
            pe.wait_ge(s_xsum, 2)
            nc.tensor.matmul(psum[:, 4, 0:F], xmean[:, :], w_ext[:, 0:F], start=True, stop=True).then_inc(s_mean, 1)
            pe.sem_inc(s_used, R)

            def product(par, r, q, t, jt):
                return nc.tensor.matmul(psum[:, 4 * par + t, 0:FV], wgt_ring[:, r, q, t * P:(t + 1) * P],
                                        vals[:, jt, 0:FV], start=(jt == 0), stop=(jt == JT - 1))

            def products(g, par):
                for n in range(C - LATE):
                    pe.wait_ge(s_wgt, g * C + (n + 1))
                    for q in range(CJ):
                        for t in range(IT):
                            op = product(par, n % R, q, t, n * CJ + q)
                    op.then_inc(s_used, 1)
                for half in range(2):
                    for n in range(C - LATE, C):
                        if half == 0:
                            pe.wait_ge(s_wgt, g * C + (n + 1))
                        for t in range(half * IT // 2, (half + 1) * IT // 2):
                            for q in range(CJ):
                                op = product(par, n % R, q, t, n * CJ + q)
                        if half == 1:
                            op.then_inc(s_used, 1)
                    if half == 0:
                        op.then_inc(s_half, 1)

            with pe.Fori(0, G // 2) as m:
                for par in range(2):
                    pe.wait_ge(s_bank[par], m + 1)
                    products(m * 2 + par, par)

            pe.wait_ge(s_flag, 1)
            with pe.If(pe.value_load(wide[0:1, 0:1]) > 0):
                def wh_tile():
                    nc.tensor.matmul(psum[:, 0, 0:FX], c_xtile, w_ext[:, :], start=True, stop=True).then_inc(c_wh, 1)

                pe.wait_ge(c_xt, 16)
                wh_tile()
                with pe.Fori(1, JT) as jt:
                    pe.wait_ge(c_xt, jt * 16 + 16)
                    pe.wait_ge(c_whsb, jt)
                    wh_tile()
                pe.wait_ge(c_set, 2)
                with pe.Fori(0, G) as g:
                    pe.wait_ge(c_xg, g * 16 + 16)
                    nc.tensor.matmul(psum[:, 4, :], wa1[:, :], c_xcols, start=True, stop=True).then_inc(c_s, 1)
                    with pe.Fori(0, JT) as jt:
                        pe.wait_ge(c_w, g * JT + jt + 1)
                        for t in range(IT):
                            op = nc.tensor.matmul(psum[:, t, 0:FV], c_wgt[:, t * P:(t + 1) * P],
                                                  vals[:, bass.ds(jt, 1), 0:FV].rearrange("p o f -> p (o f)"),
                                                  start=True, stop=True)
                        op.then_inc(c_mm, 1)


def kernel(x, adj, L0_gnn_W, L0_gnn_a):
    import numpy as np
    import concourse.bacc as bacc
    from concourse.bass_utils import run_bass_kernel_spmd

    x = np.ascontiguousarray(x)
    adj = np.asarray(adj)
    w = np.ascontiguousarray(L0_gnn_W)
    n = x.shape[0]
    rows, tiles = 512, 4
    adj_t = adj.reshape(n // rows, rows, n // (tiles * 128), tiles, 128).transpose(0, 2, 4, 3, 1)
    arrays = {
        "adj_t": np.ascontiguousarray(adj_t).reshape(-1, 128, tiles * rows),
        "x_t": np.ascontiguousarray(x.T),
        "x": x,
        "w": w,
        "w_t": np.ascontiguousarray(w.T),
        "a_t": np.ascontiguousarray(np.asarray(L0_gnn_a).reshape(2, -1).T),
    }
    nc = bacc.Bacc("TRN2", target_bir_lowering=False, num_devices=1)
    args = [nc.dram_tensor(k, v.shape, mybir.dt.from_np(v.dtype), kind="ExternalInput").ap()
            for k, v in arrays.items()]
    out = nc.dram_tensor("out", x.shape, F32, kind="ExternalOutput").ap()
    gat_norm(nc, *args, out)
    r = run_bass_kernel_spmd(nc, [arrays], core_ids=[0])
    return r.results[0]["out"]
```
